# Optimizing a Trainium2 kernel written in Bass

```python
import numpy as np
import jax
import jax.numpy as jnp

def _softmax(x, axis=-1):
    return jax.nn.softmax(x, axis=axis)

def _gelu(x):
    return jax.nn.gelu(x, approximate=True)

def _silu(x):
    return jax.nn.silu(x)

def _sigmoid(x):
    return jax.nn.sigmoid(x)

def _layernorm(x, axis=-1, eps=1e-05):
    m = jnp.mean(x, axis=axis, keepdims=True)
    v = jnp.var(x, axis=axis, keepdims=True)
    return (x - m) / jnp.sqrt(v + eps)

def _scatter_add(tgt, idx, src, axis=0):
    return tgt.at[idx].add(src)

def _segment_sum(src, seg, n):
    return jax.ops.segment_sum(src, seg, n)
kernel_name = 'mk_adaln_ffn_d1_seqx_r4_aed725'

def setup_inputs(seed: int=0):
    np.random.seed(seed)
    _w = jnp.asarray

    def _rec_inputs():
        import jax
        import jax.numpy as jnp
        _rk = jax.random.key(seed)
        x = -0.000125 + 0.9999 * jax.random.normal(jax.random.fold_in(_rk, 1), (32, 64, 1024), jnp.float32)
        _lenS = 64 - jax.random.randint(jax.random.fold_in(_rk, 7), (32,), 0, max(1, 64 // 4) + 1, jnp.int32)
        _lenS2 = 64 - jax.random.randint(jax.random.fold_in(_rk, 8), (32,), 0, max(1, 64 // 4) + 1, jnp.int32)
        cond_128 = 0.0061147 + 1.02565 * jax.random.normal(jax.random.fold_in(_rk, 11), (32, 128), jnp.float32)
        fside_S_0 = -0.022604 + 0.987366 * jax.random.normal(jax.random.fold_in(_rk, 12), (64,), jnp.float32)
        return (x, cond_128, fside_S_0)
    x, cond_128, fside_S_0 = _rec_inputs()

    def _L0_cond_setup():
        import jax, jax.numpy as jnp
        import numpy as np
        from jax import lax
        N, C_IN, L = (32, 64, 1024)
        C_OUT, K, GROUPS = (64, 9, 4)
        C_DIM, PAD, STRIDE = (128, 4, 1)
        key = jax.random.key(seed)
        k1, k2, k3, k4, k5 = jax.random.split(key, 5)
        x = jax.random.normal(k1, (N, C_IN, L), dtype=jnp.float32)
        c = jax.random.normal(k2, (N, C_DIM), dtype=jnp.float32)
        weight = jax.random.normal(k3, (C_OUT, C_IN // GROUPS, K), dtype=jnp.float32)
        c_weight = jax.random.normal(k4, (C_OUT, C_DIM), dtype=jnp.float32)
        bias = jax.random.normal(k5, (C_OUT,), dtype=jnp.float32)
        return {'x': x, 'c': c, 'weight': weight, 'c_weight': c_weight, 'bias': bias}
    _L0_cond_all = _L0_cond_setup()
    _L0_cond_in = {k: v for k, v in _L0_cond_all.items() if k in ('weight', 'c_weight')}
    del _L0_cond_all

    def _L0_ffn_setup():
        import jax, jax.numpy as jnp
        import numpy as np
        import math
        IN_DIM = 1024
        FEATURES = 1024
        BATCH, SEQ = (8, 512)
        key = jax.random.key(seed)
        kx, kk = jax.random.split(key)
        x = jax.random.normal(kx, (BATCH, SEQ, IN_DIM), dtype=jnp.float32)
        kernel = jax.random.randint(kk, (IN_DIM, FEATURES), 0, 2) > 0
        scale = jnp.asarray(1.0 / math.sqrt(IN_DIM), dtype=jnp.float32)
        return {'x': x, 'kernel': kernel, 'scale': scale}
    _L0_ffn_all = _L0_ffn_setup()
    _L0_ffn_in = {k: v for k, v in _L0_ffn_all.items() if k in ('kernel', 'scale')}
    del _L0_ffn_all
    return {'x': x, 'cond_128': cond_128, 'fside_S_0': fside_S_0, 'L0_cond_weight': _L0_cond_in['weight'], 'L0_cond_c_weight': _L0_cond_in['c_weight'], 'L0_ffn_kernel': _L0_ffn_in['kernel'], 'L0_ffn_scale': _L0_ffn_in['scale']}

def reference(x, cond_128, fside_S_0, L0_cond_weight, L0_cond_c_weight, L0_ffn_kernel, L0_ffn_scale):
    import jax
    import jax.numpy as jnp

    def _L0_cond_ref(x, c, weight, c_weight, bias):
        import jax, jax.numpy as jnp
        import numpy as np
        from jax import lax
        N, C_IN, L = (32, 64, 1024)
        C_OUT, K, GROUPS = (64, 9, 4)
        C_DIM, PAD, STRIDE = (128, 4, 1)
        out = lax.conv_general_dilated(x, weight, window_strides=(STRIDE,), padding=[(PAD, PAD)], dimension_numbers=('NCH', 'OIH', 'NCH'), feature_group_count=GROUPS)
        ctx = jnp.einsum('nd,od->no', c, c_weight)
        out = out + ctx[:, :, None] + bias[None, :, None]
        return out

    def _L0_ffn_ref(x, kernel, scale):
        import jax, jax.numpy as jnp
        import numpy as np
        import math
        IN_DIM = 1024
        FEATURES = 1024
        BATCH, SEQ = (8, 512)
        w = kernel.astype(x.dtype) * 2.0 - 1.0
        return scale * jnp.einsum('bsi,if->bsf', x, w)
    x = x + _L0_ffn_ref(_L0_cond_ref(x, cond_128, L0_cond_weight, L0_cond_c_weight, fside_S_0), L0_ffn_kernel, L0_ffn_scale)
    return x

_drawn_inputs = setup_inputs


def setup_inputs(seed=0):
    import zlib

    import numpy as np

    out = dict(_drawn_inputs(seed))
    spreads = {}
    factors = {}
    for name, (base, spread) in spreads.items():
        noise = np.random.default_rng([zlib.crc32(name.encode()), seed]).standard_normal(out[name].shape)
        drawn = base * np.exp(spread * noise) if base else spread * noise
        out[name] = jnp.asarray(drawn.astype(out[name].dtype))
    for name, factor in factors.items():
        out[name] = (out[name] * factor).astype(out[name].dtype)
    return out
```

```python
import concourse.bass as bass
from concourse import mybir
from contextlib import ExitStack

F32 = mybir.dt.float32
F32R = mybir.dt.float32r
ALU = mybir.AluOpType
ACT = mybir.ActivationFunctionType

P = 128
N, C, L = 32, 64, 1024
TAPS, PAD, GROUPS = 9, 4, 4
CG = C // GROUPS
B = P // CG
M = L // B
PAIRS = N * C // P
NG = 2 * GROUPS
HALF = NG // 2
D = 128
BANK = 512
FH = L // BANK
KP = TAPS + 2 * (B - 1)


def conv_product_kernel(nc, x, cond, bias, weight, c_weight, w_bool, scale, out):
    x_pairs = x.rearrange("(j a) c l -> j (a c) l", a=2)
    out_pairs = out.rearrange("(j a) c l -> j (a c) l", a=2)

    ctx = ExitStack()
    with ctx:
        def sb(name, shape, dt=F32):
            return ctx.enter_context(nc.sbuf_tensor(name, shape, dt))

        def ps(name, shape):
            return ctx.enter_context(nc.psum_tensor(name, shape, F32))

        def sem(name):
            return ctx.enter_context(nc.semaphore(name))

        ident = sb("ident", [P, P])
        ones = sb("ones", [P, P], F32R)
        w_bytes = sb("w_bytes", [P, B, L], mybir.dt.uint8)
        w_sign = sb("w_sign", [P, B, L], F32R)
        w_colsum = sb("w_colsum", [P, L])
        taps_nat = sb("taps_nat", [C, CG, TAPS])
        taps_pad = sb("taps_pad", [C, KP, CG])
        toeplitz = sb("toeplitz", [P, 2, GROUPS, B, CG])
        cond_nat = sb("cond_nat", [N, D])
        cw_nat = sb("cw_nat", [C, D])
        cond_t = sb("cond_t", [D, N])
        cw_t = sb("cw_t", [D, 2, C])
        bias_col = sb("bias_col", [P, 1])
        scale_col = sb("scale_col", [P, 1])
        shift = sb("shift", [P, PAIRS])
        tail_nat = sb("tail_nat", [P, CG, PAD])
        tail_blk = sb("tail_blk", [P, B, CG])
        tail_t = sb("tail_t", [P, N * GROUPS])
        x_nat = [sb(f"x_nat{s}", [P, PAD + L]) for s in range(2)]
        x_blk = [sb(f"x_blk{s}", [P, NG, B, CG]) for s in range(2)]
        x_tr = [sb(f"x_tr{s}", [P, NG, M + 1]) for s in range(2)]
        y_hi = [sb(f"y_hi{s}", [P, B, NG, CG], F32R) for s in range(2)]
        y_lo = [sb(f"y_lo{s}", [P, B, NG, CG], F32R) for s in range(2)]
        result = sb("result", [P, PAIRS, L])

        ps_t1 = ps("ps_t1", [P, B, P])
        ps_t2 = ps("ps_t2", [P, NG, M])
        ps_conv = ps("ps_conv", [P, NG, B, CG])
        ps_out = ps("ps_out", [P, FH, BANK])
        ps_toep = ps_conv[:, :, :, :].rearrange("r a b c -> r (a b c)").rearrange(
            "r (s p g o) -> r s p g o", s=2, p=B, g=GROUPS)
        ps_cond = ps_out[:, 0, 0:N]
        ps_cw = ps_out[:, 0, N:N + C]
        ps_tail = ps_out[:, 0, P:P + N * GROUPS]
        ps_ctx = ps_out[:, 1, 0:N]

        taps_in, w_in, small_in, col_in, tail_in = map(
            sem, ("taps_in", "w_in", "small_in", "col_in", "tail_in"))
        x_in = [sem(f"x_in{s}") for s in range(2)]
        ident_zero, ident_ok, taps_zero, taps_ok, ones_ok, pads_ok, tail_ok = map(
            sem, ("ident_zero", "ident_ok", "taps_zero", "taps_ok", "ones_ok", "pads_ok", "tail_ok"))
        toep_done, toep_ok, small_done, small_ok, ctx_done, shift_ok = map(
            sem, ("toep_done", "toep_ok", "small_done", "small_ok", "ctx_done", "shift_ok"))
        w_ok_act, w_ok_dve, colsum_done, colsum_ok = map(
            sem, ("w_ok_act", "w_ok_dve", "colsum_done", "colsum_ok"))
        t1_done, t2_done, conv_done, out_done = map(sem, ("t1_done", "t2_done", "conv_done", "out_done"))
        blk_ok, tr_ok, edge_ok, hi_ok, lo_ok = map(sem, ("blk_ok", "tr_ok", "edge_ok", "hi_ok", "lo_ok"))
        residual_ok, result_ok, stored = map(sem, ("residual_ok", "result_ok", "stored"))

        block = ctx.enter_context(nc.Block())

        FIRST, LAST = 1, PAIRS - 4

        def steps(eng, step):
            for i in range(-3, FIRST):
                step(i, i % 2)
            with eng.Fori(0, (LAST + 1 - FIRST) // 2) as t:
                for u in range(2):
                    step(2 * t + (FIRST + u), (FIRST + u) % 2)
            for i in range(LAST + 1, PAIRS):
                step(i, i % 2)

        def runs(j):
            return not isinstance(j, int) or 0 <= j < PAIRS

        def at(i, n):
            return isinstance(i, int) and i == n

        def reused(j):
            return not isinstance(j, int) or j >= 2

        def x_count(j, slot):
            return 16 * (j // 2 + 1) if isinstance(j, int) else 8 * (j - slot) + 16

        def row(ap, j):
            return ap[j] if isinstance(j, int) else ap[bass.ds(j, 1)].rearrange("a p l -> (a p) l")

        def line(tile, j, lo=0, hi=L):
            if isinstance(j, int):
                return tile[:, j, lo:hi]
            return tile[:, bass.ds(j, 1), lo:hi].rearrange("p a l -> p (a l)")

        @block.sync
        def _(sp):
            sp.dma_start(taps_nat[:, :, :], weight).then_inc(taps_in, 16)

            def load(j, slot):
                if reused(j):
                    sp.wait_ge(residual_ok, j - 1)
                sp.dma_start(x_nat[slot][:, PAD:PAD + L], row(x_pairs, j)).then_inc(x_in[slot], 16)

            def step(i, par):
                if runs(i + 3):
                    load(i + 3, 1 - par)
                if at(i, -3):
                    sp.dma_start(w_bytes[:, :, :], w_bool.rearrange("(m p) f -> m p f", p=B)).then_inc(w_in, 16)
                if at(i, PAIRS - 1):
                    for f in range(FH):
                        half = slice(f * BANK, (f + 1) * BANK)
                        sp.wait_ge(result_ok, FH * i + f + 1)
                        sp.dma_start(out_pairs[i][:, half], result[:, i, half]).then_inc(stored, 16)
                elif runs(i):
                    sp.wait_ge(result_ok, FH * i + FH)
                    sp.dma_start(row(out_pairs, i), line(result, i)).then_inc(stored, 16)

            steps(sp, step)
            sp.wait_ge(stored, 16 * (PAIRS + 1))

        @block.gpsimd
        def _(pool):
            nc.gpsimd.memset(ident[:, :], 0.0).then_inc(ident_zero, 1)
            pool.wait_ge(ident_zero, 1)
            nc.gpsimd.affine_select(out=ident[:, :], in_=ident[:, :], compare_op=ALU.not_equal, fill=1.0,
                                    base=0, pattern=[[-1, P]], channel_multiplier=1).then_inc(ident_ok, 1)
            nc.gpsimd.memset(ones[:, :].bitcast(F32), 1.0).then_inc(ones_ok, 1)
            pool.dma_start(tail_nat[:, :, :],
                           x.rearrange("n (g c) l -> (n g) c l", g=GROUPS)[:, :, L - PAD:L]).then_inc(tail_in, 16)
            nc.gpsimd.memset(tail_blk[:, PAD:B, :], 0.0).then_inc(tail_ok, 1)
            pool.wait_ge(tail_in, 16)
            nc.gpsimd.tensor_copy(tail_blk[:, 0:PAD, :].rearrange("r q c -> r c q"),
                                  tail_nat[:, :, :]).then_inc(tail_ok, 1)

        @block.scalar
        def _(act):
            act.dma_start(cond_nat[:, :], cond).then_inc(small_in, 16)
            act.dma_start(cw_nat[:, :], c_weight).then_inc(small_in, 16)
            act.dma_start(bias_col[0:C, :], bias).then_inc(col_in, 16)
            act.dma_start(bias_col[C:P, :], bias).then_inc(col_in, 16)
            act.dma_start(scale_col[:, :], scale.to_broadcast([P, 1])).then_inc(col_in, 16)

            for s in range(2):
                act.wait_ge(toep_done, s + 1)
                nc.scalar.copy(toeplitz[:, s].rearrange("r g p o -> r p g o"), ps_toep[:, s]).then_inc(toep_ok, 1)

            def blocks_out(j, slot):
                for h in range(2):
                    act.wait_ge(t1_done, 2 * j + h + 1)
                    if reused(j) and h == 0:
                        act.wait_ge(t2_done, 2 * j - 2)
                    q = slice(h * B // 2, (h + 1) * B // 2)
                    nc.scalar.copy(x_blk[slot][:, :, q, :].rearrange("m a q c -> m q a c"),
                                   ps_t1[:, q, :].rearrange("m q (a c) -> m q a c", c=CG)).then_inc(blk_ok, 1)

            def transposed_out(j, slot):
                for h in range(2):
                    act.wait_ge(t2_done, 2 * j + h + 1)
                    if reused(j) and h == 0:
                        act.wait_ge(conv_done, 2 * j - 2)
                    a = slice(h * HALF, (h + 1) * HALF)
                    nc.scalar.copy(x_tr[slot][:, a, 0:M], ps_t2[:, a, :]).then_inc(tr_ok, 1)

            def high_part(j, slot):
                for h in range(2):
                    act.wait_ge(conv_done, 2 * j + h + 1)
                    if reused(j) and h == 0:
                        act.wait_ge(out_done, FH * (j - 1))
                    a = slice(h * HALF, (h + 1) * HALF)
                    nc.scalar.copy(y_hi[slot][:, :, a, :].rearrange("m p a o -> m a p o"),
                                   ps_conv[:, a, :, :]).then_inc(hi_ok, 1)

            def step(i, par):
                if runs(i + 2):
                    blocks_out(i + 2, par)
                if runs(i + 1):
                    high_part(i + 1, 1 - par)
                if runs(i + 2):
                    transposed_out(i + 2, par)
                if at(i, -2):
                    act.wait_ge(w_in, 16)
                    nc.scalar.activation(w_sign[:, B // 2:B, :], w_bytes[:, B // 2:B, :], ACT.Copy,
                                         bias=-1.0, scale=2.0).then_inc(w_ok_act, 1)

            steps(act, step)

        @block.vector
        def _(dve):
            nc.vector.memset(taps_pad[:, :, :], 0.0).then_inc(taps_zero, 1)
            dve.wait_ge(taps_zero, 1)
            dve.wait_ge(taps_in, 16)
            nc.vector.tensor_copy(taps_pad[:, B - 1:B - 1 + TAPS, :].rearrange("o k c -> o c k"),
                                  taps_nat[:, :, :]).then_inc(taps_ok, 1)
            for s in range(2):
                nc.vector.memset(x_nat[s][:, 0:PAD], 0.0).then_inc(pads_ok, 1)
            dve.wait_ge(small_done, 1)
            nc.vector.tensor_copy(cond_t[:, :], ps_cond)
            for s in range(2):
                nc.vector.tensor_copy(cw_t[:, s, :], ps_cw)
            nc.vector.tensor_copy(tail_t[:, :], ps_tail).then_inc(small_ok, 1)
            dve.wait_ge(w_in, 16)
            for q in range(B // 2):
                last = nc.vector.tensor_scalar(w_sign[:, q, :], w_bytes[:, q, :], 2.0, -1.0, ALU.mult, ALU.add)
            last.then_inc(w_ok_dve, 1)
            dve.wait_ge(ctx_done, 1)
            dve.wait_ge(col_in, 48)
            for s in range(2):
                h = slice(s * C, (s + 1) * C)
                nc.vector.tensor_scalar(shift[h, :], ps_ctx[h].rearrange("r (j a) -> r a j", a=2)[:, s, :],
                                        bias_col[h, :], None, ALU.add).then_inc(shift_ok, 1)

            def edge(j, slot):
                if reused(j):
                    dve.wait_ge(conv_done, 2 * j - 2)
                a = slice(j * NG, (j + 1) * NG) if isinstance(j, int) else bass.ds(j * NG, NG)
                nc.vector.tensor_copy(x_tr[slot][:, :, M], tail_t[:, a]).then_inc(edge_ok, 1)

            def low_part(j, slot):
                for h in range(2):
                    dve.wait_ge(hi_ok, 2 * j + h + 1)
                    a = slice(h * HALF, (h + 1) * HALF)
                    nc.vector.tensor_tensor(y_lo[slot][:, :, a, :].rearrange("m p a o -> m a p o"),
                                            ps_conv[:, a, :, :],
                                            y_hi[slot][:, :, a, :].bitcast(F32).rearrange("m p a o -> m a p o"),
                                            ALU.subtract).then_inc(lo_ok, 1)

            def finish(i, f):
                dve.wait_ge(out_done, FH * i + f + 1)
                dve.wait_ge(residual_ok, i + 1)
                half = line(result, i, f * BANK, (f + 1) * BANK)
                nc.vector.scalar_tensor_tensor(half, ps_out[:, f, :], scale_col[:, :], half,
                                               ALU.mult, ALU.add).then_inc(result_ok, 1)

            def residual(j, slot):
                dve.wait_ge(t1_done, 2 * j + 2)
                nc.vector.scalar_tensor_tensor(line(result, j), w_colsum[:, :], shift_of(j),
                                               x_nat[slot][:, PAD:PAD + L],
                                               ALU.mult, ALU.add).then_inc(residual_ok, 1)

            def shift_of(j):
                return shift[:, j:j + 1] if isinstance(j, int) else shift[:, bass.ds(j, 1)]

            def colsum_out():
                for f in range(FH):
                    dve.wait_ge(colsum_done, f + 1)
                    last = nc.vector.tensor_scalar(w_colsum[:, f * BANK:(f + 1) * BANK], ps_out[:, f, :],
                                                   scale_col[:, :], None, ALU.mult)
                    last.then_inc(colsum_ok, 1)
                dve.wait_ge(colsum_ok, FH)
                dve.wait_ge(shift_ok, 2)

            def step(i, par):
                if at(i, -3):
                    colsum_out()
                if at(i, -3) or at(i, -2):
                    edge(i + 3, 1 - par)
                if runs(i):
                    finish(i, 0)
                if runs(i + 1):
                    low_part(i + 1, 1 - par)
                if runs(i):
                    finish(i, 1)
                if runs(i + 3):
                    residual(i + 3, 1 - par)
                    if not (at(i, -3) or at(i, -2)):
                        edge(i + 3, 1 - par)

            steps(dve, step)

        @block.tensor
        def _(pe):
            pe.wait_ge(ident_ok, 1)
            pe.wait_ge(taps_ok, 1)
            for s in range(2):
                for p in range(B):
                    k = (B - 1) - p + B * s
                    last = nc.tensor.transpose(ps_toep[:, s, p].rearrange("r g o -> r (g o)"),
                                               taps_pad[:, k:k + B, :].rearrange("o k c -> o (k c)"),
                                               ident[0:C, 0:C])
                last.then_inc(toep_done, 1)

            def transpose_1(j, slot):
                pe.wait_ge(x_in[slot], x_count(j, slot))
                blocks = x_nat[slot][:, 0:B * M].rearrange("r (m q) -> r q m", q=B)
                for h in range(2):
                    if not at(j, 0):
                        pe.wait_ge(blk_ok, 2 * j - 1 + h)
                    for q in range(h * B // 2, (h + 1) * B // 2):
                        last = nc.tensor.transpose(ps_t1[:, q, :], blocks[:, q, :], ident[:, :])
                    last.then_inc(t1_done, 1)

            def transpose_2(j, slot):
                for h in range(2):
                    if h == 0:
                        pe.wait_ge(blk_ok, 2 * j + 2)
                    if not at(j, 0):
                        pe.wait_ge(tr_ok, 2 * j - 1 + h)
                    for a in range(h * HALF, (h + 1) * HALF):
                        last = nc.tensor.transpose(ps_t2[:, a, :],
                                                   x_blk[slot][:, a].rearrange("m q c -> m (q c)"), ident[:, :])
                    last.then_inc(t2_done, 1)

            def conv(j, slot):
                for h in range(2):
                    pe.wait_ge(tr_ok, 2 * j + h + 1)
                    if h == 0:
                        pe.wait_ge(edge_ok, j + 1)
                    if not at(j, 0):
                        pe.wait_ge(lo_ok, 2 * j - 1 + h)
                    for g in range(GROUPS):
                        a = h * GROUPS + g
                        for s in range(2):
                            last = nc.tensor.matmul(ps_conv[:, a].rearrange("m p o -> m (p o)"),
                                                    x_tr[slot][:, a, s:s + M],
                                                    toeplitz[:, s, g].rearrange("r p o -> r (p o)"),
                                                    start=(s == 0), stop=(s == 1))
                    last.then_inc(conv_done, 1)

            def product(i, slot, f):
                if f == 0:
                    pe.wait_ge(lo_ok, 2 * i + 2)
                if not at(i, 0):
                    pe.wait_ge(result_ok, FH * i - FH + f + 1)
                for p in range(B):
                    for part in (y_hi, y_lo):
                        last = nc.tensor.matmul(ps_out[:, f, :], part[slot][:, p].rearrange("m a o -> m (a o)"),
                                                w_sign[:, p, f * BANK:(f + 1) * BANK],
                                                start=(p == 0 and part is y_hi), stop=(p == B - 1 and part is y_lo))
                last.then_inc(out_done, 1)

            def small_transposes():
                pe.wait_ge(small_in, 32)
                pe.wait_ge(tail_ok, 2)
                nc.tensor.transpose(ps_cond, cond_nat[:, :], ident[0:N, 0:N])
                nc.tensor.transpose(ps_cw, cw_nat[:, :], ident[0:C, 0:C])
                nc.tensor.transpose(ps_tail, tail_blk[:, :, :].rearrange("r q c -> r (q c)"),
                                    ident[:, :]).then_inc(small_done, 1)

            def context():
                pe.wait_ge(small_ok, 1)
                nc.tensor.matmul(ps_ctx, cw_t[:, :, :].rearrange("d s o -> d (s o)"), cond_t[:, :],
                                 start=True, stop=True).then_inc(ctx_done, 1)

            def column_sums():
                pe.wait_ge(ones_ok, 1)
                pe.wait_ge(w_ok_dve, 1)
                pe.wait_ge(w_ok_act, 1)
                pe.wait_ge(shift_ok, 2)
                for f in range(FH):
                    for p in range(B):
                        last = nc.tensor.matmul(ps_out[:, f, :], ones[:, :], w_sign[:, p, f * BANK:(f + 1) * BANK],
                                                start=(p == 0), stop=(p == B - 1))
                    last.then_inc(colsum_done, 1)

            def step(i, par):
                if at(i, -3):
                    pe.wait_ge(pads_ok, 2)
                if at(i, 0):
                    pe.wait_ge(colsum_ok, FH)
                if runs(i):
                    product(i, par, 0)
                if at(i, -1):
                    pe.wait_ge(toep_ok, 2)
                if runs(i + 1):
                    conv(i + 1, 1 - par)
                if runs(i + 2):
                    transpose_2(i + 2, par)
                if at(i, -2):
                    column_sums()
                if runs(i):
                    product(i, par, 1)
                if runs(i + 3):
                    transpose_1(i + 3, 1 - par)
                if at(i, -3):
                    small_transposes()
                    context()

            steps(pe, step)

    return nc


def kernel(x, cond_128, fside_S_0, L0_cond_weight, L0_cond_c_weight, L0_ffn_kernel, L0_ffn_scale):
    import numpy as np
    import concourse.bacc as bacc
    from concourse.bass_utils import run_bass_kernel_spmd

    nc = bacc.Bacc("TRN2", target_bir_lowering=False, num_devices=1)
    arrays = {
        "x": np.ascontiguousarray(x),
        "cond": np.ascontiguousarray(cond_128),
        "bias": np.ascontiguousarray(fside_S_0).reshape(C, 1),
        "weight": np.ascontiguousarray(L0_cond_weight),
        "c_weight": np.ascontiguousarray(L0_cond_c_weight),
        "w_bool": np.ascontiguousarray(L0_ffn_kernel),
        "scale": np.ascontiguousarray(L0_ffn_scale).reshape(1, 1),
    }
    args = [nc.dram_tensor(name, a.shape, mybir.dt.from_np(a.dtype), kind="ExternalInput").ap()
            for name, a in arrays.items()]
    out = nc.dram_tensor("out", (N, C, L), F32, kind="ExternalOutput").ap()
    conv_product_kernel(nc, *args, out)
    r = run_bass_kernel_spmd(nc, [arrays], core_ids=[0])
    return r.results[0]["out"]
```

```python
import concourse.bass as bass
from concourse import mybir
from contextlib import ExitStack

F32 = mybir.dt.float32
F32R = mybir.dt.float32r
ALU = mybir.AluOpType
ACT = mybir.ActivationFunctionType

P = 128
N, C, L = 32, 64, 1024
TAPS, PAD, GROUPS = 9, 4, 4
CG = C // GROUPS
B = P // CG
M = L // B
PITCH = 192
PAIRS = N * C // P
NG = 2 * GROUPS
HALF = NG // 2
D = 128
BANK = 512
FH = L // BANK
T = 2 * B
KP = TAPS + 2 * (B - 1)


def conv_product_kernel(nc, x, cond, bias, weight, c_weight, w_bool, scale, out):
    x_pairs = x.rearrange("(j a) c l -> j (a c) l", a=2)
    out_pairs = out.rearrange("(j a) c l -> j (a c) l", a=2)

    ctx = ExitStack()
    with ctx:
        def sb(name, shape, dt=F32):
            return ctx.enter_context(nc.sbuf_tensor(name, shape, dt))

        def ps(name, shape):
            return ctx.enter_context(nc.psum_tensor(name, shape, F32))

        def sem(name):
            return ctx.enter_context(nc.semaphore(name))

        x_phase = [sb(f"x_phase{s}", [P, B, PITCH]) for s in range(2)]
        x_blk = [sb(f"x_blk{s}", [P, NG, PITCH]) for s in range(2)]
        x_nat = [sb(f"x_nat{s}", [P, PAD + L + PAD]) for s in range(2)]
        y_hi = [sb(f"y_hi{s}", [P, B, NG, CG], F32R) for s in range(2)]
        y_lo = [sb(f"y_lo{s}", [P, B, NG, CG], F32R) for s in range(2)]
        result = sb("result", [P, PAIRS, L])
        ident = sb("ident", [C, C])
        ones = sb("ones", [P, P], F32R)
        w_bytes = sb("w_bytes", [P, B, L], mybir.dt.uint8)
        w_sign = sb("w_sign", [P, B, L], F32R)
        w_colsum = sb("w_colsum", [P, L])
        taps_nat = sb("taps_nat", [C, CG, TAPS])
        taps_pad = sb("taps_pad", [C, CG, KP])
        taps_exp = sb("taps_exp", [C, T, CG, B])
        toeplitz = sb("toeplitz", [P, 2, GROUPS, B, CG])
        cond_nat = sb("cond_nat", [N, D])
        cw_nat = sb("cw_nat", [C, D])
        cond_t = sb("cond_t", [D, N])
        cw_t = sb("cw_t", [D, 2, C])
        bias_col = sb("bias_col", [P, 1])
        scale_col = sb("scale_col", [P, 1])
        shift = sb("shift", [P, PAIRS])

        ps_conv = ps("ps_conv", [P, NG, B, CG])
        ps_out = ps("ps_out", [P, FH, BANK])
        ps_toep = ps("ps_toep", [P, 2, B, C])
        ps_cond = ps("ps_cond", [D, N])
        ps_cw = ps("ps_cw", [D, C])

        taps_in, w_in, small_in, col_in = map(sem, ("taps_in", "w_in", "small_in", "col_in"))
        x_in = [sem(f"x_in{s}") for s in range(2)]
        blk_in = [[sem(f"blk_in{s}_{h}") for h in range(2)] for s in range(2)]
        ident_zero, ident_ok, taps_zero, taps_ok, ones_ok, pads_ok = map(
            sem, ("ident_zero", "ident_ok", "taps_zero", "taps_ok", "ones_ok", "pads_ok"))
        exp_ok_act, exp_ok_dve, toep_done, toep_ok, small_done, small_ok, ctx_done, shift_ok = map(
            sem, ("exp_ok_act", "exp_ok_dve", "toep_done", "toep_ok", "small_done", "small_ok",
                  "ctx_done", "shift_ok"))
        w_ok_act, w_ok_dve, colsum_done, colsum_ok = map(
            sem, ("w_ok_act", "w_ok_dve", "colsum_done", "colsum_ok"))
        conv_done, out_done, phase_ok, hi_ok, lo_ok, residual_ok, result_ok, stored = map(
            sem, ("conv_done", "out_done", "phase_ok", "hi_ok", "lo_ok", "residual_ok", "result_ok", "stored"))

        block = ctx.enter_context(nc.Block())

        FIRST, LAST = 1, PAIRS - 4

        def steps(eng, step):
            for i in range(-3, FIRST):
                step(i, i % 2)
            with eng.Fori(0, (LAST + 1 - FIRST) // 2) as t:
                for u in range(2):
                    step(2 * t + (FIRST + u), (FIRST + u) % 2)
            for i in range(LAST + 1, PAIRS):
                step(i, i % 2)

        def runs(j):
            return not isinstance(j, int) or 0 <= j < PAIRS

        def at(i, n):
            return isinstance(i, int) and i == n

        def reused(j):
            return not isinstance(j, int) or j >= 2

        def x_count(j, slot):
            return 16 * (j // 2 + 1) if isinstance(j, int) else 8 * (j - slot) + 16

        def blk_count(j, slot):
            return GROUPS * x_count(j, slot)

        def row(ap, j):
            return ap[j] if isinstance(j, int) else ap[bass.ds(j, 1)].rearrange("a p l -> (a p) l")

        def line(tile, j, lo=0, hi=L):
            if isinstance(j, int):
                return tile[:, j, lo:hi]
            return tile[:, bass.ds(j, 1), lo:hi].rearrange("p a l -> p (a l)")

        @block.sync
        def _(sp):
            def load(j, slot):
                if reused(j):
                    sp.wait_ge(residual_ok, j - 1)
                sp.dma_start(x_nat[slot][:, PAD:PAD + L], row(x_pairs, j)).then_inc(x_in[slot], 16)

            def to_blocks(j, slot):
                if reused(j):
                    sp.wait_ge(conv_done, 2 * j - 2)
                sp.wait_ge(phase_ok, j + 1)
                for a in range(NG):
                    sp.dma_start(x_blk[slot][:, a, 0:M + 1],
                                 x_phase[slot][a * CG:(a + 1) * CG, :, 0:M + 1]
                                 ).then_inc(blk_in[slot][a // GROUPS], 16)

            def step(i, par):
                if at(i, -3):
                    sp.dma_start(taps_nat[:, :, :], weight).then_inc(taps_in, 16)
                if runs(i + 3):
                    load(i + 3, 1 - par)
                if at(i, -3):
                    sp.dma_start(w_bytes[:, :, :], w_bool.rearrange("(m p) f -> m p f", p=B)).then_inc(w_in, 16)
                if runs(i + 2):
                    to_blocks(i + 2, par)
                if at(i, PAIRS - 1):
                    for f in range(FH):
                        half = slice(f * BANK, (f + 1) * BANK)
                        sp.wait_ge(result_ok, FH * i + f + 1)
                        sp.dma_start(out_pairs[i][:, half], result[:, i, half]).then_inc(stored, 16)
                elif runs(i):
                    sp.wait_ge(result_ok, FH * i + FH)
                    sp.dma_start(row(out_pairs, i), line(result, i)).then_inc(stored, 16)

            steps(sp, step)
            sp.wait_ge(stored, 16 * (PAIRS + 1))

        @block.gpsimd
        def _(pool):
            nc.gpsimd.memset(ident[:, :], 0.0).then_inc(ident_zero, 1)
            pool.wait_ge(ident_zero, 1)
            nc.gpsimd.affine_select(out=ident[:, :], in_=ident[:, :], compare_op=ALU.not_equal, fill=1.0,
                                    base=0, pattern=[[-1, C]], channel_multiplier=1).then_inc(ident_ok, 1)
            for s in range(2):
                nc.gpsimd.memset(x_nat[s][:, 0:PAD], 0.0).then_inc(pads_ok, 1)
                nc.gpsimd.memset(x_nat[s][:, PAD + L:PAD + L + PAD], 0.0).then_inc(pads_ok, 1)
            nc.gpsimd.memset(ones[:, :].bitcast(F32), 1.0).then_inc(ones_ok, 1)

        def expand_taps(copy, qs):
            for q in qs:
                last = copy(taps_exp[:, :, :, q], taps_pad[:, :, q:q + T].rearrange("o c t -> o t c"))
            return last

        @block.scalar
        def _(act):
            act.dma_start(cond_nat[:, :], cond).then_inc(small_in, 16)
            act.dma_start(cw_nat[:, :], c_weight).then_inc(small_in, 16)
            act.dma_start(bias_col[0:C, :], bias).then_inc(col_in, 16)
            act.dma_start(bias_col[C:P, :], bias).then_inc(col_in, 16)
            act.dma_start(scale_col[:, :], scale.to_broadcast([P, 1])).then_inc(col_in, 16)
            act.wait_ge(taps_ok, 1)
            expand_taps(nc.scalar.copy, range(B // 2)).then_inc(exp_ok_act, 1)

            def to_phases(j, slot):
                act.wait_ge(x_in[slot], x_count(j, slot))
                if at(j, 0):
                    act.wait_ge(pads_ok, 4)
                if reused(j):
                    for h in range(2):
                        act.wait_ge(blk_in[slot][h], blk_count(j - 2, slot))
                nc.scalar.copy(x_phase[slot][:, :, 0:M + 1],
                               x_nat[slot][:, :].rearrange("r (m q) -> r q m", q=B)).then_inc(phase_ok, 1)

            def high_part(j, slot):
                for h in range(2):
                    act.wait_ge(conv_done, 2 * j + h + 1)
                    if reused(j) and h == 0:
                        act.wait_ge(out_done, FH * (j - 1))
                    a = slice(h * HALF, (h + 1) * HALF)
                    nc.scalar.copy(y_hi[slot][:, :, a, :].rearrange("m u a o -> m a u o"),
                                   ps_conv[:, a, :, :]).then_inc(hi_ok, 1)

            def step(i, par):
                if runs(i + 1):
                    high_part(i + 1, 1 - par)
                if runs(i + 3):
                    to_phases(i + 3, 1 - par)
                if at(i, -3):
                    for s in range(2):
                        act.wait_ge(toep_done, s + 1)
                        nc.scalar.copy(toeplitz[:, s].rearrange("r g u o -> r u g o"),
                                       ps_toep[:, s].rearrange("r u (g o) -> r u g o", g=GROUPS)
                                       ).then_inc(toep_ok, 1)
                if at(i, -2):
                    act.wait_ge(w_in, 16)
                    nc.scalar.activation(w_sign[:, B // 2:B, :], w_bytes[:, B // 2:B, :], ACT.Copy,
                                         bias=-1.0, scale=2.0).then_inc(w_ok_act, 1)

            steps(act, step)

        @block.vector
        def _(dve):
            nc.vector.memset(taps_pad[:, :, :], 0.0).then_inc(taps_zero, 1)
            dve.wait_ge(taps_zero, 1)
            dve.wait_ge(taps_in, 16)
            nc.vector.tensor_copy(taps_pad[:, :, B - 1:B - 1 + TAPS], taps_nat[:, :, :]).then_inc(taps_ok, 1)
            dve.wait_ge(taps_ok, 1)
            expand_taps(nc.vector.tensor_copy, range(B // 2, B)).then_inc(exp_ok_dve, 1)
            dve.wait_ge(small_done, 1)
            nc.vector.tensor_copy(cond_t[:, :], ps_cond[:, :])
            for s in range(2):
                last = nc.vector.tensor_copy(cw_t[:, s, :], ps_cw[:, :])
            last.then_inc(small_ok, 1)
            dve.wait_ge(w_in, 16)
            for p in range(B // 2):
                last = nc.vector.tensor_scalar(w_sign[:, p, :], w_bytes[:, p, :], 2.0, -1.0, ALU.mult, ALU.add)
            last.then_inc(w_ok_dve, 1)
            dve.wait_ge(ctx_done, 1)
            dve.wait_ge(col_in, 48)
            for s in range(2):
                h = slice(s * C, (s + 1) * C)
                nc.vector.tensor_scalar(shift[h, :], ps_cond[h, :].rearrange("r (j a) -> r a j", a=2)[:, s, :],
                                        bias_col[h, :], None, ALU.add).then_inc(shift_ok, 1)
            for f in range(FH):
                dve.wait_ge(colsum_done, f + 1)
                nc.vector.tensor_scalar(w_colsum[:, f * BANK:(f + 1) * BANK], ps_out[:, f, :],
                                        scale_col[:, :], None, ALU.mult).then_inc(colsum_ok, 1)
            dve.wait_ge(colsum_ok, FH)
            dve.wait_ge(shift_ok, 2)

            def low_part(j, slot):
                for h in range(2):
                    dve.wait_ge(hi_ok, 2 * j + h + 1)
                    a = slice(h * HALF, (h + 1) * HALF)
                    nc.vector.tensor_tensor(y_lo[slot][:, :, a, :].rearrange("m u a o -> m a u o"),
                                            ps_conv[:, a, :, :],
                                            y_hi[slot][:, :, a, :].bitcast(F32).rearrange("m u a o -> m a u o"),
                                            ALU.subtract).then_inc(lo_ok, 1)

            def finish(i, f):
                dve.wait_ge(out_done, FH * i + f + 1)
                dve.wait_ge(residual_ok, i + 1)
                half = line(result, i, f * BANK, (f + 1) * BANK)
                nc.vector.scalar_tensor_tensor(half, ps_out[:, f, :], scale_col[:, :], half,
                                               ALU.mult, ALU.add).then_inc(result_ok, 1)

            def residual(j, slot):
                dve.wait_ge(phase_ok, j + 1)
                shift_j = shift[:, j:j + 1] if isinstance(j, int) else shift[:, bass.ds(j, 1)]
                nc.vector.scalar_tensor_tensor(line(result, j), w_colsum[:, :], shift_j,
                                               x_nat[slot][:, PAD:PAD + L],
                                               ALU.mult, ALU.add).then_inc(residual_ok, 1)

            def step(i, par):
                if runs(i):
                    finish(i, 0)
                if runs(i + 1):
                    low_part(i + 1, 1 - par)
                if runs(i):
                    finish(i, 1)
                if runs(i + 3):
                    residual(i + 3, 1 - par)

            steps(dve, step)

        @block.tensor
        def _(pe):
            pe.wait_ge(ident_ok, 1)
            pe.wait_ge(small_in, 32)
            nc.tensor.transpose(ps_cond[:, :], cond_nat[:, :], ident[0:N, 0:N])
            nc.tensor.transpose(ps_cw[:, :], cw_nat[:, :], ident[:, :]).then_inc(small_done, 1)
            pe.wait_ge(exp_ok_act, 1)
            pe.wait_ge(exp_ok_dve, 1)
            for s in range(2):
                for u in range(B):
                    last = nc.tensor.transpose(ps_toep[:, s, u], taps_exp[:, B * s + u].rearrange("o c q -> o (c q)"),
                                               ident[:, :])
                last.then_inc(toep_done, 1)
            pe.wait_ge(small_ok, 1)
            nc.tensor.matmul(ps_cond[:, :], cw_t[:, :, :].rearrange("d s o -> d (s o)"), cond_t[:, :],
                             start=True, stop=True).then_inc(ctx_done, 1)
            pe.wait_ge(ones_ok, 1)
            pe.wait_ge(w_ok_dve, 1)
            pe.wait_ge(w_ok_act, 1)
            for f in range(FH):
                for p in range(B):
                    last = nc.tensor.matmul(ps_out[:, f, :], ones[:, :], w_sign[:, p, f * BANK:(f + 1) * BANK],
                                            start=(p == 0), stop=(p == B - 1))
                last.then_inc(colsum_done, 1)

            def conv(j, slot):
                for h in range(2):
                    pe.wait_ge(blk_in[slot][h], blk_count(j, slot))
                    if not at(j, 0):
                        pe.wait_ge(lo_ok, 2 * j - 1 + h)
                    for g in range(GROUPS):
                        a = h * GROUPS + g
                        for s in range(2):
                            last = nc.tensor.matmul(ps_conv[:, a].rearrange("m u o -> m (u o)"),
                                                    x_blk[slot][:, a, s:s + M],
                                                    toeplitz[:, s, g].rearrange("r u o -> r (u o)"),
                                                    start=(s == 0), stop=(s == 1))
                    last.then_inc(conv_done, 1)

            def product(i, slot, f):
                if f == 0:
                    pe.wait_ge(lo_ok, 2 * i + 2)
                if not at(i, 0):
                    pe.wait_ge(result_ok, FH * i - FH + f + 1)
                for u in range(B):
                    for part in (y_hi, y_lo):
                        last = nc.tensor.matmul(ps_out[:, f, :], part[slot][:, u].rearrange("m a o -> m (a o)"),
                                                w_sign[:, B - 1 - u, f * BANK:(f + 1) * BANK],
                                                start=(u == 0 and part is y_hi), stop=(u == B - 1 and part is y_lo))
                last.then_inc(out_done, 1)

            def step(i, par):
                if at(i, 0):
                    pe.wait_ge(colsum_ok, FH)
                if runs(i):
                    product(i, par, 0)
                if at(i, -1):
                    pe.wait_ge(toep_ok, 2)
                if runs(i + 1):
                    conv(i + 1, 1 - par)
                if runs(i):
                    product(i, par, 1)

            steps(pe, step)

    return nc


def kernel(x, cond_128, fside_S_0, L0_cond_weight, L0_cond_c_weight, L0_ffn_kernel, L0_ffn_scale):
    import numpy as np
    import concourse.bacc as bacc
    from concourse.bass_utils import run_bass_kernel_spmd

    nc = bacc.Bacc("TRN2", target_bir_lowering=False, num_devices=1)
    arrays = {
        "x": np.ascontiguousarray(x),
        "cond": np.ascontiguousarray(cond_128),
        "bias": np.ascontiguousarray(fside_S_0).reshape(C, 1),
        "weight": np.ascontiguousarray(L0_cond_weight),
        "c_weight": np.ascontiguousarray(L0_cond_c_weight),
        "w_bool": np.ascontiguousarray(L0_ffn_kernel),
        "scale": np.ascontiguousarray(L0_ffn_scale).reshape(1, 1),
    }
    args = [nc.dram_tensor(name, a.shape, mybir.dt.from_np(a.dtype), kind="ExternalInput").ap()
            for name, a in arrays.items()]
    out = nc.dram_tensor("out", (N, C, L), F32, kind="ExternalOutput").ap()
    conv_product_kernel(nc, *args, out)
    r = run_bass_kernel_spmd(nc, [arrays], core_ids=[0])
    return r.results[0]["out"]
```

```python
import concourse.bass as bass
from concourse import mybir
from contextlib import ExitStack

F32 = mybir.dt.float32
F32R = mybir.dt.float32r
ALU = mybir.AluOpType
ACT = mybir.ActivationFunctionType

P = 128
N, C, L = 32, 64, 1024
TAPS, PAD, GROUPS = 9, 4, 4
CG = C // GROUPS
B = P // CG
M = L // B
PITCH = 192
PAIRS = N * C // P
NG = 2 * GROUPS
HALF = NG // 2
D = 128
BANK = 512
FH = L // BANK
PIECE = BANK // 2
WARM = 5, 1, 7, 3
SHIFT_AT = 2
W_DVE = 5
T = 2 * B
KP = TAPS + 2 * (B - 1)


def conv_product_kernel(nc, x, cond, bias, weight, c_weight, w_bool, scale, shift_dram, out):
    x_pairs = x.rearrange("(j a) c l -> j (a c) l", a=2)
    out_pairs = out.rearrange("(j a) c l -> j (a c) l", a=2)

    ctx = ExitStack()
    with ctx:
        def sb(name, shape, dt=F32):
            return ctx.enter_context(nc.sbuf_tensor(name, shape, dt))

        def ps(name, shape):
            return ctx.enter_context(nc.psum_tensor(name, shape, F32))

        def sem(name):
            return ctx.enter_context(nc.semaphore(name))

        x_phase = [sb(f"x_phase{s}", [P, B, PITCH]) for s in range(2)]
        x_blk = [sb(f"x_blk{s}", [P, NG, PITCH]) for s in range(2)]
        y_sum = [sb(f"y_sum{s}", [P, NG, B, CG]) for s in range(2)]
        y_hi = [sb(f"y_hi{s}", [P, B, NG, CG], F32R) for s in range(2)]
        y_lo = [sb(f"y_lo{s}", [P, B, NG, CG], F32R) for s in range(2)]
        x_nat = sb("x_nat", [P, PAIRS, PAD + L + PAD])
        ident = sb("ident", [C, C])
        w_bytes = sb("w_bytes", [P, B, L], mybir.dt.uint8)
        w_sign = sb("w_sign", [P, B, L], F32R)
        taps_nat = sb("taps_nat", [C, CG, TAPS])
        taps_pad = sb("taps_pad", [C, CG, KP])
        taps_exp = sb("taps_exp", [C, T, CG, B])
        toeplitz = sb("toeplitz", [P, 2, GROUPS, B, CG])
        warm = sb("warm", [P, BANK], mybir.dt.bfloat16)
        cond_nat = sb("cond_nat", [N, D])
        cw_nat = sb("cw_nat", [C, D])
        cond_t = sb("cond_t", [D, N])
        cw_t = sb("cw_t", [D, C])
        bias_rows = sb("bias_rows", [N, C])
        shift_rows = sb("shift_rows", [N, C])
        shift = sb("shift", [P, PAIRS, NG, CG])
        scale_col = sb("scale_col", [P, 1])

        ps_conv = ps("ps_conv", [P, NG, B, CG])
        ps_out = ps("ps_out", [P, FH, BANK])
        ps_toep = ps("ps_toep", [P, 2, B, C])
        ps_toep_flat = ps_toep[:, 0].rearrange("r u o -> r (u o)")
        ps_cond = ps("ps_cond", [D, N])
        ps_cw = ps("ps_cw", [D, C])
        ps_ctx = ps_out[0:N, 1, 0:C]

        taps_in, small_in, bias_in, scale_in, shift_in = map(
            sem, ("taps_in", "small_in", "bias_in", "scale_in", "shift_in"))
        w_in, shift_in_0, warm_ok = map(sem, ("w_in", "shift_in_0", "warm_ok"))
        blk_in_pool = sem("blk_in_pool")
        x_in = [sem(f"x_in{s}") for s in range(2)]
        blk_in = [[sem(f"blk_in{s}_{h}") for h in range(2)] for s in range(2)]
        ident_zero, ident_ok, taps_zero, taps_ok, pads_ok = map(
            sem, ("ident_zero", "ident_ok", "taps_zero", "taps_ok", "pads_ok"))
        exp_ok, toep_done, toep_ok, small_done, small_ok, ctx_done, shift_ok, shift_out = map(
            sem, ("exp_ok", "toep_done", "toep_ok", "small_done", "small_ok", "ctx_done", "shift_ok", "shift_out"))
        w_ok_act, w_ok_dve = map(sem, ("w_ok_act", "w_ok_dve"))
        conv_done, out_done, phase_ok, sum_ok, hi_ok, lo_ok, result_ok, stored = map(
            sem, ("conv_done", "out_done", "phase_ok", "sum_ok", "hi_ok", "lo_ok", "result_ok", "stored"))

        block = ctx.enter_context(nc.Block())

        FIRST, LAST = 1, PAIRS - 4

        def steps(eng, step):
            for i in range(-3, FIRST):
                step(i, i % 2)
            with eng.Fori(0, (LAST + 1 - FIRST) // 2) as t:
                for u in range(2):
                    step(2 * t + (FIRST + u), (FIRST + u) % 2)
            for i in range(LAST + 1, PAIRS):
                step(i, i % 2)

        def runs(j):
            return not isinstance(j, int) or 0 <= j < PAIRS

        def at(i, n):
            return isinstance(i, int) and i == n

        def reused(j):
            return not isinstance(j, int) or j >= 2

        def x_count(j, slot):
            return 16 * (j // 2 + 1) if isinstance(j, int) else 8 * (j - slot) + 16

        def wait_blocks(eng, j, slot, h):
            if at(j, 0) and h == 1:
                eng.wait_ge(blk_in_pool, 16 * GROUPS)
            else:
                eng.wait_ge(blk_in[slot][h], GROUPS * (x_count(j, slot) - (16 if (slot, h) == (0, 1) else 0)))

        def rows_of(j, h):
            if at(j, 0) and h == 1:
                return [(slice(0, B // 2), 1), (slice(B // 2, B), 1)]
            return [(slice(0, B), 2)]

        def y_count(j, h, u=slice(0, B)):
            return 4 * j + 2 * h + u.stop * 2 // B

        def row(ap, j):
            return ap[j] if isinstance(j, int) else ap[bass.ds(j, 1)].rearrange("a p l -> (a p) l")

        def line(j, lo, hi):
            if isinstance(j, int):
                return x_nat[:, j, lo:hi]
            return x_nat[:, bass.ds(j, 1), lo:hi].rearrange("p a l -> p (a l)")

        def positions(f):
            return PAD + f * BANK, PAD + (f + 1) * BANK

        def last_positions(f):
            lo, hi = ((0, BANK), (BANK, BANK + PIECE), (BANK + PIECE, L))[f]
            return PAD + lo, PAD + hi

        def to_block(eng, slot, a, landed):
            eng.dma_start(x_blk[slot][:, a, 0:M + 1], x_phase[slot][a * CG:(a + 1) * CG, :, 0:M + 1]
                          ).then_inc(landed, 16)

        @block.sync
        def _(sp):
            def load(j, slot):
                sp.dma_start(line(j, PAD, PAD + L), row(x_pairs, j)).then_inc(x_in[slot], 16)

            def to_blocks(j, slot):
                if reused(j):
                    sp.wait_ge(conv_done, 2 * j - 2)
                sp.wait_ge(phase_ok, j + 1)
                for a in range(GROUPS if at(j, 0) else NG):
                    to_block(sp, slot, a, blk_in[slot][a // GROUPS])

            def step(i, par):
                if at(i, -3):
                    load(0, 0)
                    sp.dma_start(taps_nat[:, :, :], weight).then_inc(taps_in, 16)
                    sp.dma_start(w_bytes[:, :, :], w_bool.rearrange("(m p) f -> m p f", p=B)).then_inc(w_in, 16)
                elif at(i, -2):
                    to_blocks(0, 0)
                    load(1, 1)
                elif at(i, -1):
                    to_blocks(1, 1)
                    load(2, 0)
                else:
                    if runs(i + 3):
                        load(i + 3, 1 - par)
                    if runs(i + 2):
                        to_blocks(i + 2, par)
                if at(i, PAIRS - 1):
                    for f in range(FH + 1):
                        lo, hi = last_positions(f)
                        sp.wait_ge(result_ok, FH * i + f + 1)
                        sp.dma_start(out_pairs[i][:, lo - PAD:hi - PAD], line(i, lo, hi)).then_inc(stored, 16)
                elif runs(i):
                    sp.wait_ge(result_ok, FH * i + FH)
                    sp.dma_start(row(out_pairs, i), line(i, PAD, PAD + L)).then_inc(stored, 16)

            steps(sp, step)
            sp.wait_ge(stored, 16 * (PAIRS + 2))

        @block.gpsimd
        def _(pool):
            pool.dma_start(bias_rows[:, :], bias.to_broadcast([N, C])).then_inc(bias_in, 16)
            nc.gpsimd.memset(ident[:, :], 0.0).then_inc(ident_zero, 1)
            pool.wait_ge(ident_zero, 1)
            nc.gpsimd.affine_select(out=ident[:, :], in_=ident[:, :], compare_op=ALU.not_equal, fill=1.0,
                                    base=0, pattern=[[-1, C]], channel_multiplier=1).then_inc(ident_ok, 1)
            nc.gpsimd.memset(warm[:, :], 0.0).then_inc(warm_ok, 1)
            nc.gpsimd.memset(x_nat[:, :, 0:PAD], 0.0).then_inc(pads_ok, 1)
            nc.gpsimd.memset(x_nat[:, :, PAD + L:PAD + L + PAD], 0.0).then_inc(pads_ok, 1)
            pool.dma_start(scale_col[:, :], scale.to_broadcast([P, 1])).then_inc(scale_in, 16)
            pool.wait_ge(phase_ok, 1)
            for a in range(GROUPS, NG):
                to_block(pool, 0, a, blk_in_pool)

        @block.scalar
        def _(act):
            act.dma_start(cond_nat[:, :], cond).then_inc(small_in, 16)
            act.dma_start(cw_nat[:, :], c_weight).then_inc(small_in, 16)
            act.wait_ge(small_done, 2)
            nc.scalar.copy(cond_t[:, :], ps_cond[:, :]).then_inc(small_ok, 1)
            nc.scalar.copy(cw_t[:, :], ps_cw[:, :]).then_inc(small_ok, 1)

            def signs(f):
                c = slice(f * BANK, (f + 1) * BANK)
                nc.scalar.activation(w_sign[:, W_DVE:B, c], w_bytes[:, W_DVE:B, c], ACT.Copy,
                                     bias=-1.0, scale=2.0).then_inc(w_ok_act, 1)

            def to_phases(j, slot):
                act.wait_ge(x_in[slot], x_count(j, slot))
                if at(j, 2):
                    act.wait_ge(pads_ok, 2)
                if reused(j):
                    for h in range(2):
                        wait_blocks(act, j - 2, slot, h)
                nc.scalar.copy(x_phase[slot][:, :, 0:M + 1],
                               line(j, 0, PAD + L + PAD).rearrange("r (m q) -> r q m", q=B)).then_inc(phase_ok, 1)

            def high_part(j, slot):
                for h in range(2):
                    if reused(j) and h == 0:
                        act.wait_ge(out_done, FH * (j - 1))
                    a = slice(h * HALF, (h + 1) * HALF)
                    for u, halves in rows_of(j, h):
                        act.wait_ge(sum_ok, y_count(j, h, u))
                        nc.scalar.copy(y_hi[slot][:, u, a, :].rearrange("m u a o -> m a u o"),
                                       y_sum[slot][:, a, u, :]).then_inc(hi_ok, halves)

            def step(i, par):
                if at(i, -3):
                    act.wait_ge(shift_ok, 1)
                    act.dma_start(shift_dram.rearrange("a (n o) -> (a n) o", n=N), shift_rows[:, :]
                                  ).then_inc(shift_out, 16)
                    for s in range(2):
                        act.wait_ge(toep_done, s + 1)
                        nc.scalar.copy(toeplitz[:, s].rearrange("r g u o -> r u g o"),
                                       ps_toep[:, s].rearrange("r u (g o) -> r u g o", g=GROUPS)
                                       ).then_inc(toep_ok, 1)
                    act.wait_ge(shift_out, 16)
                    flat = shift[:, :, :, :].rearrange("p j a o -> p (j a o)")
                    act.dma_start(flat[:, 0:P], shift_dram[:, 0:P].to_broadcast([P, P])).then_inc(shift_in_0, 16)
                    act.dma_start(flat[:, P:N * C], shift_dram[:, P:N * C].to_broadcast([P, N * C - P])
                                  ).then_inc(shift_in, 16)
                    act.wait_ge(w_in, 16)
                    for f in range(FH):
                        signs(f)
                if runs(i + 1):
                    high_part(i + 1, 1 - par)
                if runs(i + 3) and not at(i, -3) and not at(i, -2):
                    to_phases(i + 3, 1 - par)

            steps(act, step)

        @block.vector
        def _(dve):
            nc.vector.memset(taps_pad[:, :, :], 0.0).then_inc(taps_zero, 1)
            dve.wait_ge(taps_zero, 1)

            def first_phases(j):
                dve.wait_ge(x_in[j], 16)
                if j == 0:
                    dve.wait_ge(pads_ok, 2)
                nc.vector.tensor_copy(x_phase[j][:, :, 0:M + 1],
                                      x_nat[:, j, :].rearrange("r (m q) -> r q m", q=B)).then_inc(phase_ok, 1)

            first_phases(0)
            dve.wait_ge(taps_in, 16)
            nc.vector.tensor_copy(taps_pad[:, :, B - 1:B - 1 + TAPS], taps_nat[:, :, :]).then_inc(taps_ok, 1)
            dve.wait_ge(taps_ok, 1)
            for q in range(B):
                if q == SHIFT_AT:
                    dve.wait_ge(ctx_done, 1)
                    dve.wait_ge(bias_in, 16)
                    nc.vector.tensor_tensor(shift_rows[:, :], ps_ctx, bias_rows[:, :], ALU.add).then_inc(shift_ok, 1)
                nc.vector.tensor_copy(taps_exp[:, :, :, q],
                                      taps_pad[:, :, q:q + T].rearrange("o c t -> o t c")).then_inc(exp_ok, 1)
            dve.wait_ge(w_in, 16)
            for f in range(FH):
                c = slice(f * BANK, (f + 1) * BANK)
                nc.vector.tensor_scalar(w_sign[:, 0:W_DVE, c], w_bytes[:, 0:W_DVE, c], 2.0, -1.0,
                                        ALU.mult, ALU.add).then_inc(w_ok_dve, 1)
            first_phases(1)

            def add_shift(j, slot):
                for h in range(2):
                    dve.wait_ge(conv_done, 2 * j + h + 1)
                    if at(j, 0) and h == 0:
                        dve.wait_ge(shift_in_0, 16)
                    if at(j, 1) and h == 0:
                        dve.wait_ge(shift_in, 16)
                    if reused(j):
                        dve.wait_ge(lo_ok, 2 * j - 3 + h)
                    a = slice(h * HALF, (h + 1) * HALF)
                    if isinstance(j, int):
                        shift_j = shift[:, j, a, :]
                    else:
                        shift_j = shift[:, bass.ds(j, 1), a, :].rearrange("m j a o -> m (j a) o")
                    for u, halves in rows_of(j, h):
                        nc.vector.tensor_tensor(y_sum[slot][:, a, u, :], ps_conv[:, a, u, :],
                                                shift_j.unsqueeze(2).to_broadcast([P, HALF, u.stop - u.start, CG]),
                                                ALU.add).then_inc(sum_ok, halves)

            def low_part(j, slot):
                for h in range(2):
                    dve.wait_ge(hi_ok, y_count(j, h))
                    a = slice(h * HALF, (h + 1) * HALF)
                    nc.vector.tensor_tensor(y_lo[slot][:, :, a, :].rearrange("m u a o -> m a u o"),
                                            y_sum[slot][:, a, :, :],
                                            y_hi[slot][:, :, a, :].bitcast(F32).rearrange("m u a o -> m a u o"),
                                            ALU.subtract).then_inc(lo_ok, 1)

            def finish(i, f):
                dve.wait_ge(out_done, FH * i + f + 1)
                if at(i, 0) and f == 0:
                    dve.wait_ge(scale_in, 16)
                if at(i, PAIRS - 1) and f > 0:
                    product = ps_out[:, 1, 0:PIECE] if f < FH else ps_toep_flat[:, 0:PIECE]
                    there = line(i, *last_positions(f))
                else:
                    product = ps_out[:, f, :]
                    there = line(i, *positions(f))
                nc.vector.scalar_tensor_tensor(there, product, scale_col[:, :], there,
                                               ALU.mult, ALU.add).then_inc(result_ok, 1)

            def step(i, par):
                if runs(i):
                    finish(i, 0)
                if runs(i + 1):
                    add_shift(i + 1, 1 - par)
                    low_part(i + 1, 1 - par)
                if runs(i):
                    finish(i, 1)
                if at(i, PAIRS - 1):
                    finish(i, FH)

            steps(dve, step)

        @block.tensor
        def _(pe):
            def keep_busy(count):
                for _ in range(count):
                    nc.tensor.matmul(ps_out[:, 0, :], warm[:, 0:P], warm[:, :], start=True, stop=True)

            pe.wait_ge(warm_ok, 1)
            keep_busy(WARM[0])
            pe.wait_ge(ident_ok, 1)
            pe.wait_ge(small_in, 32)
            nc.tensor.transpose(ps_cond[:, :], cond_nat[:, :], ident[0:N, 0:N]).then_inc(small_done, 1)
            nc.tensor.transpose(ps_cw[:, :], cw_nat[:, :], ident[:, :]).then_inc(small_done, 1)
            keep_busy(WARM[1])
            pe.wait_ge(small_ok, 2)
            nc.tensor.matmul(ps_ctx, cond_t[:, :], cw_t[:, :], start=True, stop=True).then_inc(ctx_done, 1)

            keep_busy(WARM[2])
            pe.wait_ge(exp_ok, B)
            for s in range(2):
                for u in range(B):
                    last = nc.tensor.transpose(ps_toep[:, s, u], taps_exp[:, B * s + u].rearrange("o c q -> o (c q)"),
                                               ident[:, :])
                last.then_inc(toep_done, 1)
            keep_busy(WARM[3])

            def conv(j, slot):
                for h in range(2):
                    wait_blocks(pe, j, slot, h)
                    if not at(j, 0):
                        pe.wait_ge(sum_ok, y_count(j - 1, h))
                    for g in range(GROUPS):
                        a = h * GROUPS + g
                        for s in range(2):
                            last = nc.tensor.matmul(ps_conv[:, a].rearrange("m u o -> m (u o)"),
                                                    x_blk[slot][:, a, s:s + M],
                                                    toeplitz[:, s, g].rearrange("r u o -> r (u o)"),
                                                    start=(s == 0), stop=(s == 1))
                    last.then_inc(conv_done, 1)

            def product(i, slot, f):
                if at(i, PAIRS - 1) and f == FH - 1:
                    pieces = [(ps_out[:, f, 0:PIECE], f * BANK), (ps_toep_flat[:, 0:PIECE], f * BANK + PIECE)]
                else:
                    pieces = [(ps_out[:, f, :], f * BANK)]
                if f == 0:
                    pe.wait_ge(hi_ok, y_count(i, 1, rows_of(i, 1)[0][0]))
                if not at(i, 0):
                    pe.wait_ge(result_ok, FH * i - FH + f + 1)
                if at(i, 0):
                    pe.wait_ge(w_ok_act, f + 1)
                    pe.wait_ge(w_ok_dve, f + 1)
                for dest, c in pieces:
                    for part in (y_hi, y_lo):
                        if f == 0 and part is y_lo:
                            pe.wait_ge(lo_ok, 2 * i + 2)
                        for u in range(B):
                            if at(i, 0) and f == 0 and part is y_hi and u == B // 2:
                                pe.wait_ge(hi_ok, y_count(i, 1))
                            last = nc.tensor.matmul(dest, part[slot][:, u].rearrange("m a o -> m (a o)"),
                                                    w_sign[:, B - 1 - u, c:c + dest.shape[-1]],
                                                    start=(u == 0 and part is y_hi),
                                                    stop=(u == B - 1 and part is y_lo))
                    last.then_inc(out_done, 1)

            def step(i, par):
                if runs(i):
                    product(i, par, 0)
                if at(i, -1):
                    pe.wait_ge(toep_ok, 2)
                if runs(i + 1):
                    conv(i + 1, 1 - par)
                if runs(i):
                    product(i, par, 1)

            steps(pe, step)

    return nc


def kernel(x, cond_128, fside_S_0, L0_cond_weight, L0_cond_c_weight, L0_ffn_kernel, L0_ffn_scale):
    import numpy as np
    import concourse.bacc as bacc
    from concourse.bass_utils import run_bass_kernel_spmd

    nc = bacc.Bacc("TRN2", target_bir_lowering=False, num_devices=1)
    arrays = {
        "x": np.ascontiguousarray(x),
        "cond": np.ascontiguousarray(cond_128),
        "bias": np.ascontiguousarray(fside_S_0).reshape(1, C),
        "weight": np.ascontiguousarray(L0_cond_weight),
        "c_weight": np.ascontiguousarray(L0_cond_c_weight),
        "w_bool": np.ascontiguousarray(L0_ffn_kernel),
        "scale": np.ascontiguousarray(L0_ffn_scale).reshape(1, 1),
    }
    args = [nc.dram_tensor(name, a.shape, mybir.dt.from_np(a.dtype), kind="ExternalInput").ap()
            for name, a in arrays.items()]
    shift_dram = nc.dram_tensor("shift_dram", (1, N * C), F32, kind="Internal").ap()
    out = nc.dram_tensor("out", (N, C, L), F32, kind="ExternalOutput").ap()
    conv_product_kernel(nc, *args, shift_dram, out)
    r = run_bass_kernel_spmd(nc, [arrays], core_ids=[0])
    return r.results[0]["out"]
```
